# Optimizing a Trainium2 kernel written in Bass

```python
import numpy as np
import jax
import jax.numpy as jnp

def _softmax(x, axis=-1):
    return jax.nn.softmax(x, axis=axis)

def _gelu(x):
    return jax.nn.gelu(x, approximate=True)

def _silu(x):
    return jax.nn.silu(x)

def _sigmoid(x):
    return jax.nn.sigmoid(x)

def _layernorm(x, axis=-1, eps=1e-05):
    m = jnp.mean(x, axis=axis, keepdims=True)
    v = jnp.var(x, axis=axis, keepdims=True)
    return (x - m) / jnp.sqrt(v + eps)

def _scatter_add(tgt, idx, src, axis=0):
    return tgt.at[idx].add(src)

def _segment_sum(src, seg, n):
    return jax.ops.segment_sum(src, seg, n)
kernel_name = 'mk_dlrm_tower_d1_rec_r8_b513ad'

def setup_inputs(seed: int=0):
    np.random.seed(seed)
    _w = jnp.asarray

    def _rec_inputs():
        import jax
        import jax.numpy as jnp
        _tk = jax.random.key(seed)
        dense_ctx = jax.random.normal(jax.random.fold_in(_tk, 190), (2048, 16), jnp.float32)
        ids = jnp.stack([jax.random.randint(jax.random.fold_in(_tk, 200 + f), (2048,), 0, v, jnp.int32) for f, v in enumerate([125000, 125000, 125000, 1000, 1000, 1250, 1250, 12500, 1250, 12500, 1250, 1250, 1250, 1250, 1000, 1000, 12500, 12500, 12500, 1000, 1250, 1250, 12500, 1250, 1250, 1000, 12500, 1250, 1250, 1000, 1000, 1000, 1000, 1000, 1250, 1250, 1000, 1000, 1250, 1000])], axis=1)
        tbl_0 = 0.05 * jax.random.normal(jax.random.fold_in(_tk, 500 + 0), (125000, 64), jnp.float32)
        tbl_1 = 0.05 * jax.random.normal(jax.random.fold_in(_tk, 500 + 1), (125000, 64), jnp.float32)
        tbl_2 = 0.05 * jax.random.normal(jax.random.fold_in(_tk, 500 + 2), (125000, 64), jnp.float32)
        tbl_3 = 0.05 * jax.random.normal(jax.random.fold_in(_tk, 500 + 3), (1000, 64), jnp.float32)
        tbl_4 = 0.05 * jax.random.normal(jax.random.fold_in(_tk, 500 + 4), (1000, 64), jnp.float32)
        tbl_5 = 0.05 * jax.random.normal(jax.random.fold_in(_tk, 500 + 5), (1250, 64), jnp.float32)
        tbl_6 = 0.05 * jax.random.normal(jax.random.fold_in(_tk, 500 + 6), (1250, 64), jnp.float32)
        tbl_7 = 0.05 * jax.random.normal(jax.random.fold_in(_tk, 500 + 7), (12500, 64), jnp.float32)
        tbl_8 = 0.05 * jax.random.normal(jax.random.fold_in(_tk, 500 + 8), (1250, 64), jnp.float32)
        tbl_9 = 0.05 * jax.random.normal(jax.random.fold_in(_tk, 500 + 9), (12500, 64), jnp.float32)
        tbl_10 = 0.05 * jax.random.normal(jax.random.fold_in(_tk, 500 + 10), (1250, 64), jnp.float32)
        tbl_11 = 0.05 * jax.random.normal(jax.random.fold_in(_tk, 500 + 11), (1250, 64), jnp.float32)
        tbl_12 = 0.05 * jax.random.normal(jax.random.fold_in(_tk, 500 + 12), (1250, 64), jnp.float32)
        tbl_13 = 0.05 * jax.random.normal(jax.random.fold_in(_tk, 500 + 13), (1250, 64), jnp.float32)
        tbl_14 = 0.05 * jax.random.normal(jax.random.fold_in(_tk, 500 + 14), (1000, 64), jnp.float32)
        tbl_15 = 0.05 * jax.random.normal(jax.random.fold_in(_tk, 500 + 15), (1000, 64), jnp.float32)
        tbl_16 = 0.05 * jax.random.normal(jax.random.fold_in(_tk, 500 + 16), (12500, 64), jnp.float32)
        tbl_17 = 0.05 * jax.random.normal(jax.random.fold_in(_tk, 500 + 17), (12500, 64), jnp.float32)
        tbl_18 = 0.05 * jax.random.normal(jax.random.fold_in(_tk, 500 + 18), (12500, 64), jnp.float32)
        tbl_19 = 0.05 * jax.random.normal(jax.random.fold_in(_tk, 500 + 19), (1000, 64), jnp.float32)
        tbl_20 = 0.05 * jax.random.normal(jax.random.fold_in(_tk, 500 + 20), (1250, 64), jnp.float32)
        tbl_21 = 0.05 * jax.random.normal(jax.random.fold_in(_tk, 500 + 21), (1250, 64), jnp.float32)
        tbl_22 = 0.05 * jax.random.normal(jax.random.fold_in(_tk, 500 + 22), (12500, 64), jnp.float32)
        tbl_23 = 0.05 * jax.random.normal(jax.random.fold_in(_tk, 500 + 23), (1250, 64), jnp.float32)
        tbl_24 = 0.05 * jax.random.normal(jax.random.fold_in(_tk, 500 + 24), (1250, 64), jnp.float32)
        tbl_25 = 0.05 * jax.random.normal(jax.random.fold_in(_tk, 500 + 25), (1000, 64), jnp.float32)
        tbl_26 = 0.05 * jax.random.normal(jax.random.fold_in(_tk, 500 + 26), (12500, 64), jnp.float32)
        tbl_27 = 0.05 * jax.random.normal(jax.random.fold_in(_tk, 500 + 27), (1250, 64), jnp.float32)
        tbl_28 = 0.05 * jax.random.normal(jax.random.fold_in(_tk, 500 + 28), (1250, 64), jnp.float32)
        tbl_29 = 0.05 * jax.random.normal(jax.random.fold_in(_tk, 500 + 29), (1000, 64), jnp.float32)
        tbl_30 = 0.05 * jax.random.normal(jax.random.fold_in(_tk, 500 + 30), (1000, 64), jnp.float32)
        tbl_31 = 0.05 * jax.random.normal(jax.random.fold_in(_tk, 500 + 31), (1000, 64), jnp.float32)
        tbl_32 = 0.05 * jax.random.normal(jax.random.fold_in(_tk, 500 + 32), (1000, 64), jnp.float32)
        tbl_33 = 0.05 * jax.random.normal(jax.random.fold_in(_tk, 500 + 33), (1000, 64), jnp.float32)
        tbl_34 = 0.05 * jax.random.normal(jax.random.fold_in(_tk, 500 + 34), (1250, 64), jnp.float32)
        tbl_35 = 0.05 * jax.random.normal(jax.random.fold_in(_tk, 500 + 35), (1250, 64), jnp.float32)
        tbl_36 = 0.05 * jax.random.normal(jax.random.fold_in(_tk, 500 + 36), (1000, 64), jnp.float32)
        tbl_37 = 0.05 * jax.random.normal(jax.random.fold_in(_tk, 500 + 37), (1000, 64), jnp.float32)
        tbl_38 = 0.05 * jax.random.normal(jax.random.fold_in(_tk, 500 + 38), (1250, 64), jnp.float32)
        tbl_39 = 0.05 * jax.random.normal(jax.random.fold_in(_tk, 500 + 39), (1000, 64), jnp.float32)
        _rk = jax.random.fold_in(_tk, 7)
        W_top1 = 0.0354441 * jax.random.normal(jax.random.fold_in(_tk, 801), (796, 512), jnp.float32)
        W_top2 = 0.0441942 * jax.random.normal(jax.random.fold_in(_tk, 802), (512, 256), jnp.float32)
        W_top3 = 0.0625 * jax.random.normal(jax.random.fold_in(_tk, 803), (256, 1), jnp.float32)
        b_top1 = jnp.zeros((512,), jnp.float32)
        b_top2 = jnp.zeros((256,), jnp.float32)
        return (dense_ctx, ids, tbl_0, tbl_1, tbl_2, tbl_3, tbl_4, tbl_5, tbl_6, tbl_7, tbl_8, tbl_9, tbl_10, tbl_11, tbl_12, tbl_13, tbl_14, tbl_15, tbl_16, tbl_17, tbl_18, tbl_19, tbl_20, tbl_21, tbl_22, tbl_23, tbl_24, tbl_25, tbl_26, tbl_27, tbl_28, tbl_29, tbl_30, tbl_31, tbl_32, tbl_33, tbl_34, tbl_35, tbl_36, tbl_37, tbl_38, tbl_39, W_top1, b_top1, W_top2, b_top2, W_top3)
    dense_ctx, ids, tbl_0, tbl_1, tbl_2, tbl_3, tbl_4, tbl_5, tbl_6, tbl_7, tbl_8, tbl_9, tbl_10, tbl_11, tbl_12, tbl_13, tbl_14, tbl_15, tbl_16, tbl_17, tbl_18, tbl_19, tbl_20, tbl_21, tbl_22, tbl_23, tbl_24, tbl_25, tbl_26, tbl_27, tbl_28, tbl_29, tbl_30, tbl_31, tbl_32, tbl_33, tbl_34, tbl_35, tbl_36, tbl_37, tbl_38, tbl_39, W_top1, b_top1, W_top2, b_top2, W_top3 = _rec_inputs()

    def _L0_rec_setup():
        import jax, jax.numpy as jnp
        import numpy as np
        B, N, E = (1024, 40, 64)
        P = N * (N - 1) // 2

        def _pair_indices(n):
            row, col = ([], [])
            for i in range(n - 1):
                for j in range(i + 1, n):
                    row.append(i)
                    col.append(j)
            return (np.asarray(row), np.asarray(col))
        key = jax.random.key(seed)
        k1, k2 = jax.random.split(key)
        inputs = jax.random.normal(k1, (B, N, E), dtype=jnp.float32)
        std = float(np.sqrt(2.0 / (E + E)))
        param = jax.random.normal(k2, (E, P, E), dtype=jnp.float32) * std
        return {'inputs': inputs, 'param': param}
    _L0_rec_all = _L0_rec_setup()
    _L0_rec_in = {k: v for k, v in _L0_rec_all.items() if k in ('param',)}
    del _L0_rec_all
    return {'dense_ctx': dense_ctx, 'ids': ids, 'tbl_0': tbl_0, 'tbl_1': tbl_1, 'tbl_2': tbl_2, 'tbl_3': tbl_3, 'tbl_4': tbl_4, 'tbl_5': tbl_5, 'tbl_6': tbl_6, 'tbl_7': tbl_7, 'tbl_8': tbl_8, 'tbl_9': tbl_9, 'tbl_10': tbl_10, 'tbl_11': tbl_11, 'tbl_12': tbl_12, 'tbl_13': tbl_13, 'tbl_14': tbl_14, 'tbl_15': tbl_15, 'tbl_16': tbl_16, 'tbl_17': tbl_17, 'tbl_18': tbl_18, 'tbl_19': tbl_19, 'tbl_20': tbl_20, 'tbl_21': tbl_21, 'tbl_22': tbl_22, 'tbl_23': tbl_23, 'tbl_24': tbl_24, 'tbl_25': tbl_25, 'tbl_26': tbl_26, 'tbl_27': tbl_27, 'tbl_28': tbl_28, 'tbl_29': tbl_29, 'tbl_30': tbl_30, 'tbl_31': tbl_31, 'tbl_32': tbl_32, 'tbl_33': tbl_33, 'tbl_34': tbl_34, 'tbl_35': tbl_35, 'tbl_36': tbl_36, 'tbl_37': tbl_37, 'tbl_38': tbl_38, 'tbl_39': tbl_39, 'W_top1': W_top1, 'b_top1': b_top1, 'W_top2': W_top2, 'b_top2': b_top2, 'W_top3': W_top3, 'L0_rec_param': _L0_rec_in['param']}

def reference(dense_ctx, ids, tbl_0, tbl_1, tbl_2, tbl_3, tbl_4, tbl_5, tbl_6, tbl_7, tbl_8, tbl_9, tbl_10, tbl_11, tbl_12, tbl_13, tbl_14, tbl_15, tbl_16, tbl_17, tbl_18, tbl_19, tbl_20, tbl_21, tbl_22, tbl_23, tbl_24, tbl_25, tbl_26, tbl_27, tbl_28, tbl_29, tbl_30, tbl_31, tbl_32, tbl_33, tbl_34, tbl_35, tbl_36, tbl_37, tbl_38, tbl_39, W_top1, b_top1, W_top2, b_top2, W_top3, L0_rec_param):
    import jax
    import jax.numpy as jnp

    def _L0_rec_ref(inputs, param):
        import jax, jax.numpy as jnp
        import numpy as np
        B, N, E = (1024, 40, 64)
        P = N * (N - 1) // 2

        def _pair_indices(n):
            row, col = ([], [])
            for i in range(n - 1):
                for j in range(i + 1, n):
                    row.append(i)
                    col.append(j)
            return (np.asarray(row), np.asarray(col))
        n = inputs.shape[1]
        rowidx, colidx = _pair_indices(n)
        p = inputs[:, rowidx]
        q = inputs[:, colidx]
        out = jnp.einsum('bie,fie,bif->bi', p, param, q)
        return out[:, None, :]
    e = jnp.stack([tbl_0[ids[:, 0]], tbl_1[ids[:, 1]], tbl_2[ids[:, 2]], tbl_3[ids[:, 3]], tbl_4[ids[:, 4]], tbl_5[ids[:, 5]], tbl_6[ids[:, 6]], tbl_7[ids[:, 7]], tbl_8[ids[:, 8]], tbl_9[ids[:, 9]], tbl_10[ids[:, 10]], tbl_11[ids[:, 11]], tbl_12[ids[:, 12]], tbl_13[ids[:, 13]], tbl_14[ids[:, 14]], tbl_15[ids[:, 15]], tbl_16[ids[:, 16]], tbl_17[ids[:, 17]], tbl_18[ids[:, 18]], tbl_19[ids[:, 19]], tbl_20[ids[:, 20]], tbl_21[ids[:, 21]], tbl_22[ids[:, 22]], tbl_23[ids[:, 23]], tbl_24[ids[:, 24]], tbl_25[ids[:, 25]], tbl_26[ids[:, 26]], tbl_27[ids[:, 27]], tbl_28[ids[:, 28]], tbl_29[ids[:, 29]], tbl_30[ids[:, 30]], tbl_31[ids[:, 31]], tbl_32[ids[:, 32]], tbl_33[ids[:, 33]], tbl_34[ids[:, 34]], tbl_35[ids[:, 35]], tbl_36[ids[:, 36]], tbl_37[ids[:, 37]], tbl_38[ids[:, 38]], tbl_39[ids[:, 39]]], axis=1)
    z = _L0_rec_ref(e, L0_rec_param)
    z = z.reshape(z.shape[0], -1)
    h = jnp.concatenate([z, dense_ctx], axis=1)
    h = jnp.maximum(h @ W_top1 + b_top1, 0.0)
    h = jnp.maximum(h @ W_top2 + b_top2, 0.0)
    y = h @ W_top3
    return y

_drawn_inputs = setup_inputs


def setup_inputs(seed=0):
    import zlib

    import numpy as np

    out = dict(_drawn_inputs(seed))
    spreads = {'b_top1': (0.0, 0.1), 'b_top2': (0.0, 0.1)}
    factors = {}
    for name, (base, spread) in spreads.items():
        noise = np.random.default_rng([zlib.crc32(name.encode()), seed]).standard_normal(out[name].shape)
        drawn = base * np.exp(spread * noise) if base else spread * noise
        out[name] = jnp.asarray(drawn.astype(out[name].dtype))
    for name, factor in factors.items():
        out[name] = (out[name] * factor).astype(out[name].dtype)
    return out
```

```python
from contextlib import ExitStack

import concourse.bass as bass
from concourse import mybir

F32 = mybir.dt.float32
F32R = mybir.dt.float32r
I32 = mybir.dt.int32
ALU = mybir.AluOpType
ACT = mybir.ActivationFunctionType

P = 128
E = 64
FIELDS = 40
BATCH = 2048
DENSE = 16
H1, H2 = 512, 256
TILES = FIELDS // 2
NB = 512
CHUNKS = BATCH // NB
BT = NB // P

UNITS = [(m, k) for m in range(TILES) for k in range(m + 1)]
NU = len(UNITS)
BLOCKS = [(u, jj, k == m) for u, (m, k) in enumerate(UNITS) for jj in ((0, 1) if k < m else (1,))]
NBLK = len(BLOCKS)
BLOCKS_OF = [[b for b, (v, _, _) in enumerate(BLOCKS) if v == u] for u in range(NU)]

PIECE = 10
NPIECE = NBLK // PIECE
PW = PIECE * P
RAW_SLOTS, W_SLOTS = 2, 4
G_SLOTS = 10
Q_SLOTS = 5
T_SLOTS = 3
PROD_SLOTS = 6
LAG = 2

ZB = 64
ZT = -(-NBLK // ZB)
DENSE_ROW = 16
GROUPS = 4
START = 1

HEAD_TILES = 4
HEAD_PIECES = 3
HEAD_GATHERS = 8
LAST = NU - TILES
HEAD_AT = [LAST + 6 + 3 * t for t in range(HEAD_TILES)]
SUB_DELAY = 2


def pair(i, j):
    return i * FIELDS - i * (i + 1) // 2 + j - i - 1


def z_row(b):
    t, v = divmod(b, ZB)
    return t, 32 * (v % GROUPS) + 2 * (v // GROUPS)


def first_unit(m):
    return m * (m + 1) // 2


def units_through_piece(n):
    return BLOCKS[PIECE * (n + 1) - 1][0] + 1 if n >= 0 else 0


def sums_before(u):
    return -(-(BLOCKS_OF[u][-1] + 1) // GROUPS) * GROUPS if u >= 0 else 0


def prep_step(m):
    return max(s for s in range(m) if m * m - s * s >= 9)


def prep_plan():
    transposes, splits = {}, {}
    for m in range(HEAD_TILES, TILES):
        s = prep_step(m)
        transposes.setdefault(first_unit(s), []).append(m)
        splits.setdefault(min(first_unit(s) + SUB_DELAY, first_unit(m)), []).append(m)
    return transposes, splits


def gather_plan():
    tasks = []
    for m in range(HEAD_GATHERS, TILES):
        tasks.append((prep_step(m) ** 2 - 28, "gather", m))
    for n in range(HEAD_PIECES, NPIECE):
        tasks.append((PIECE * (n - HEAD_PIECES) + 1, "split", n))
    for m in range(HEAD_GATHERS):
        tasks.append((345 + 7 * m, "gather", TILES + m))
    for n in range(HEAD_PIECES):
        tasks.append((PIECE * (NPIECE + n - HEAD_PIECES) + 1, "split", NPIECE + n))
    tasks.sort(key=lambda x: x[0])
    return [(kind, n) for _, kind, n in tasks]


def bilinear_tower(nc, tables, idx, dense_t, weights, w1z, b1c, w2p, b2c, w3c, out):
    prep_before, split_before = prep_plan()

    with ExitStack() as ctx:
        def sb(name, shape, dt=F32):
            return ctx.enter_context(nc.sbuf_tensor(name, shape, dt))

        def ps(name, shape):
            return ctx.enter_context(nc.psum_tensor(name, shape, F32))

        def sem(name):
            return ctx.enter_context(nc.semaphore(name))

        idx_all = sb("idx_all", [P, CHUNKS, FIELDS * BT], I32)
        idx_now = sb("idx_now", [P, FIELDS * BT], I32)
        rows = sb("rows", [P, G_SLOTS, BT, 2 * E])
        e_t = sb("e_t", [P, TILES, NB])
        q_even = sb("q_even", [P, Q_SLOTS, NB], F32R)
        q_odd = sb("q_odd", [P, Q_SLOTS, NB], F32R)
        w_raw = sb("w_raw", [P, RAW_SLOTS, PW])
        w_hi = sb("w_hi", [P, W_SLOTS, PW], F32R)
        w_lo = sb("w_lo", [P, W_SLOTS, PW], F32R)
        prod = sb("prod", [P, PROD_SLOTS, 2, NB])
        z_t = sb("z_t", [P, ZT, NB])
        w1 = sb("w1", [P, ZT, H1])
        w2 = sb("w2", [P, H1 // P, H2])
        w3 = sb("w3", [P, H2 // P])
        b1 = sb("b1", [P, H1 // P])
        b2 = sb("b2", [P, H2 // P])
        h1 = sb("h1", [P, H1 // P, NB])
        h2 = sb("h2", [P, H2 // P, NB])
        y = sb("y", [1, NB])
        dense = sb("dense", [DENSE, NB])
        ident = sb("ident", [P, P])
        strip = sb("strip", [P, 62])
        place = sb("place", [DENSE, 32])

        t_ps = [ps(f"t_ps{i}", [P, 2, NB]) for i in range(T_SLOTS)]
        z_ps = ps("z_ps", [P, NB])
        tr_ps = ps("tr_ps", [P, NB])

        consts = sem("consts")
        strip_written = sem("strip_written")
        idx_in = sem("idx_in")
        mlp_in = sem("mlp_in")
        idx_copied = sem("idx_copied")
        slot_reused = sem("slot_reused")
        gathered = [sem(f"gathered{i}") for i in range(G_SLOTS)]
        raw_in = [sem(f"raw_in{i}") for i in range(RAW_SLOTS)]
        dense_in = sem("dense_in")
        w_hi_ready = sem("w_hi_ready")
        w_lo_ready = sem("w_lo_ready")
        transposed = sem("transposed")
        q_hi_ready = sem("q_hi_ready")
        q_ready = sem("q_ready")
        t_ready = sem("t_ready")
        t_free = sem("t_free")
        summed = sem("summed")
        dense_placed = sem("dense_placed")
        z_copied = sem("z_copied")
        h1_ps = sem("h1_ps")
        h1_ready = sem("h1_ready")
        h2_ps = sem("h2_ps")
        h2_ready = sem("h2_ready")
        y_ps = sem("y_ps")
        y_ready = sem("y_ready")
        y_out = sem("y_out")

        block = ctx.enter_context(nc.Block())

        @block.sync
        def _(sp):
            def load_piece(c, n):
                cols = weights[:, (n % NPIECE) * PW:(n % NPIECE + 1) * PW]
                for half in range(2):
                    sp.dma_start(w_raw[E * half:E * half + E, n % RAW_SLOTS, :], cols).then_inc(
                        raw_in[n % RAW_SLOTS], 16)

            sp.dma_start(idx_all[:, :, :], idx).then_inc(idx_in, 16)
            for n in range(RAW_SLOTS):
                load_piece(0, n)
            for dst, src in ((b1[:, :], b1c), (b2[:, :], b2c), (w3[:, :], w3c), (w2[:, :, :], w2p),
                             (w1[:, :, :], w1z)):
                sp.dma_start(dst, src).then_inc(mlp_in, 16)
            with sp.Fori(0, CHUNKS) as c:
                for n in range(RAW_SLOTS, NPIECE):
                    sp.wait_ge(w_lo_ready, c * NPIECE + n - RAW_SLOTS + 1)
                    load_piece(c, n)
                with sp.If(c < CHUNKS - 1):
                    for n in range(NPIECE, NPIECE + RAW_SLOTS):
                        sp.wait_ge(w_lo_ready, c * NPIECE + n - RAW_SLOTS + 1)
                        load_piece(c, n)

        @block.gpsimd
        def _(pool):
            nc.gpsimd.memset(ident[:, :], 0.0).then_inc(consts, 1)
            nc.gpsimd.memset(place[:, :], 0.0).then_inc(consts, 1)
            pool.wait_ge(consts, 2)
            nc.gpsimd.affine_select(out=ident[:, :], in_=ident[:, :], compare_op=ALU.not_equal, fill=1.0,
                                    base=0, pattern=[[-1, P]], channel_multiplier=1).then_inc(consts, 1)
            nc.gpsimd.affine_select(out=place[:, :], in_=place[:, :], compare_op=ALU.not_equal, fill=1.0,
                                    base=DENSE_ROW, pattern=[[-1, 32]], channel_multiplier=1).then_inc(consts, 1)

            def copy_indices(c):
                nc.gpsimd.tensor_copy(idx_now[:, :], idx_all[:, c, :]).then_inc(idx_copied, 1)
                pool.wait_ge(idx_copied, c + 1)

            def gather(c, m, slot_taken):
                slot = m % G_SLOTS
                if slot_taken:
                    pool.wait_ge(transposed, c * TILES + m - G_SLOTS + 1)
                    pool.sem_inc(slot_reused, 1)
                for f in range(2):
                    for t in range(BT):
                        col = ((m % TILES) * 2 + f) * BT + t
                        nc.gpsimd.indirect_dma_start(
                            out=rows[:, slot, t, E * f:E * f + E], out_offset=None, in_=tables[(m % TILES) * 2 + f],
                            in_offset=bass.IndirectOffsetOnAxis(ap=idx_now[:, col:col + 1], axis=0),
                        ).then_inc(gathered[slot], 16)

            def split(c, n):
                pool.wait_ge(w_hi_ready, c * NPIECE + n + 1)
                nc.gpsimd.tensor_tensor(w_lo[:, n % W_SLOTS, :], w_raw[:, n % RAW_SLOTS, :],
                                        w_hi[:, n % W_SLOTS, :].bitcast(F32), ALU.subtract).then_inc(w_lo_ready, 1)

            plan = gather_plan()
            inner = [t for t in plan if t[1] < (TILES if t[0] == "gather" else NPIECE)]
            ahead = [t for t in plan if t not in inner]
            body, tail = plan[:plan.index(ahead[0])], plan[plan.index(ahead[0]):]
            assert not any(t[0] == "gather" and t in inner for t in tail)

            pool.wait_ge(idx_in, 16)
            nc.gpsimd.tensor_copy(idx_now[:, :], idx_all[:, 0, :]).then_inc(idx_copied, 1)
            pool.wait_ge(idx_copied, 1)
            for kind, n in [("gather", 0), ("split", 0), ("gather", 1), ("gather", 2), ("gather", 3),
                            ("split", 1), ("gather", 4), ("split", 2)] + [
                                ("gather", m) for m in range(5, HEAD_GATHERS)]:
                if kind == "gather":
                    gather(0, n, False)
                else:
                    split(0, n)
            with pool.Fori(0, CHUNKS) as c:
                for kind, n in body:
                    if kind == "gather":
                        gather(c, n, n >= G_SLOTS)
                    else:
                        split(c, n)
                with pool.If(c < CHUNKS - 1):
                    for slot in range(G_SLOTS):
                        pool.wait_ge(gathered[slot], (c + 1) * (TILES // G_SLOTS) * 2 * BT * 16)
                    copy_indices(nc.s_assert_within(c + 1, 1, CHUNKS - 1))
                for kind, n in tail:
                    if n < NPIECE and kind == "split":
                        split(c, n)
                        continue
                    with pool.If(c < CHUNKS - 1):
                        if kind == "gather":
                            gather(c, n, True)
                        else:
                            split(c, n)

        @block.scalar
        def _(act):
            def round_weights(c, n, slot_taken):
                act.wait_ge(raw_in[n % RAW_SLOTS], (c * (NPIECE // RAW_SLOTS) + n // RAW_SLOTS + 1) * 32)
                if slot_taken:
                    act.wait_ge(t_ready, START + c * NU + units_through_piece(n - W_SLOTS))
                nc.scalar.activation(w_hi[:, n % W_SLOTS, :], w_raw[:, n % RAW_SLOTS, :],
                                     ACT.Copy).then_inc(w_hi_ready, 1)

            def prepare(c, m, slot_taken):
                act.wait_ge(transposed, c * TILES + m + 1)
                if m >= TILES:
                    act.wait_ge(t_free, c * NU + (LAST + m - TILES) + 1 + T_SLOTS)
                tile, slot = m % TILES, m % Q_SLOTS
                nc.scalar.activation(e_t[:, tile, :], tr_ps[:, :], ACT.Copy)
                if slot_taken:
                    act.wait_ge(t_ready, START + c * NU + first_unit(m - Q_SLOTS + 1))
                nc.scalar.activation(q_even[0:E, slot, :], tr_ps[0:E, :], ACT.Copy)
                nc.scalar.activation(q_odd[E:P, slot, :], tr_ps[E:P, :], ACT.Copy).then_inc(q_hi_ready, 1)

            def copy_z(c, t):
                if t < ZT - 1:
                    act.wait_ge(summed, START + c * NBLK + (t + 1) * ZB)
                else:
                    act.wait_ge(dense_placed, START + c + 1)
                nc.scalar.activation(z_t[:, t, :], z_ps[:, :], ACT.Copy).then_inc(z_copied, 1)

            def tower(c):
                for h in range(H1 // P):
                    act.wait_ge(h1_ps, c * (H1 // P) + h + 1)
                    nc.scalar.activation(h1[:, h, :], t_ps[h // 2][:, h % 2, :], ACT.Relu,
                                         bias=b1[:, h:h + 1]).then_inc(h1_ready, 1)
                for h in range(H2 // P):
                    act.wait_ge(h2_ps, c * (H2 // P) + h + 1)
                    nc.scalar.activation(h2[:, h, :], t_ps[2][:, h, :], ACT.Relu,
                                         bias=b2[:, h:h + 1]).then_inc(h2_ready, 1)
                act.wait_ge(y_ps, c + 1)
                nc.scalar.activation(y[:, :], t_ps[2][0:1, 0, :], ACT.Copy).then_inc(y_ready, 1)
                act.wait_ge(y_ready, START + c + 1)
                act.dma_start(out[:, bass.ds(c * NB, NB)], y[:, :]).then_inc(y_out, 16)
                act.wait_ge(y_out, (c + 1) * 16)

            act.sem_inc(z_copied, START)
            act.sem_inc(y_ready, START)
            for n in range(HEAD_PIECES):
                round_weights(0, n, False)
            for m in range(HEAD_TILES):
                prepare(0, m, False)
            act.wait_ge(mlp_in, 5 * 16)
            with act.Fori(0, CHUNKS) as c:
                act.wait_ge(dense_placed, START + c)
                act.dma_start(dense[:, :], dense_t[:, bass.ds(c * NB, NB)]).then_inc(dense_in, 16)
                for u, (m, k) in enumerate(UNITS):
                    for tile in prep_before.get(u, ()):
                        prepare(c, tile, tile >= Q_SLOTS)
                    if u in HEAD_AT:
                        with act.If(c < CHUNKS - 1):
                            prepare(c, TILES + HEAD_AT.index(u), True)
                    for b in BLOCKS_OF[u]:
                        if b % PIECE == 0:
                            n = b // PIECE + HEAD_PIECES
                            if n < NPIECE:
                                round_weights(c, n, True)
                            else:
                                with act.If(c < CHUNKS - 1):
                                    round_weights(c, n, True)
                    for b in BLOCKS_OF[max(u - LAG - 1, 0)]:
                        if u > LAG and b % ZB == ZB - 1:
                            copy_z(c, b // ZB)
                copy_z(c, ZT - 1)
                tower(c)

        @block.vector
        def _(dve):
            dve.sem_inc(t_free, T_SLOTS)
            nc.vector.memset(strip[:, :], 0.0).then_inc(strip_written, 1)
            dve.wait_ge(strip_written, 1)
            nc.vector.memset(strip[0:E, 30:31], 1.0).then_inc(strip_written, 1)
            nc.vector.memset(strip[E:P, 31:32], 1.0).then_inc(strip_written, 1)

            def remainders(c, m):
                tile, slot = m % TILES, m % Q_SLOTS
                dve.wait_ge(q_hi_ready, c * TILES + m + 1)
                nc.vector.tensor_tensor(q_even[E:P, slot, :], e_t[0:E, tile, :],
                                        q_even[0:E, slot, :].bitcast(F32), ALU.subtract)
                nc.vector.tensor_tensor(q_odd[0:E, slot, :], e_t[E:P, tile, :],
                                        q_odd[E:P, slot, :].bitcast(F32), ALU.subtract).then_inc(q_ready, 1)

            for m in range(HEAD_TILES):
                remainders(0, m)
            with dve.Fori(0, CHUNKS) as c:
                for u, (m, k) in enumerate(UNITS):
                    for tile in split_before.get(u, ()):
                        remainders(c, tile)
                    if u - SUB_DELAY in HEAD_AT:
                        with dve.If(c < CHUNKS - 1):
                            remainders(c, TILES + HEAD_AT.index(u - SUB_DELAY))
                    dve.wait_ge(t_ready, START + c * NU + u + 1)
                    dve.wait_ge(summed, START + c * NBLK + sums_before(u - PROD_SLOTS))
                    dst, src = prod[:, u % PROD_SLOTS, :, :], t_ps[u % T_SLOTS]
                    if k < m:
                        nc.vector.tensor_tensor(dst, src[:, :, :],
                                                e_t[:, k, :].unsqueeze(1).broadcast_to([P, 2, NB]),
                                                ALU.mult).then_inc(t_free, 1)
                    else:
                        nc.vector.tensor_tensor(dst[0:E, 1, :], src[0:E, 1, :], e_t[0:E, k, :],
                                                ALU.mult).then_inc(t_free, 1)

        @block.tensor
        def _(pe):
            for s in (t_ready, summed, dense_placed):
                pe.sem_inc(s, START)
            pe.wait_ge(consts, 4)
            pe.wait_ge(strip_written, 3)

            def transpose_tile(c, m, ps_taken):
                slot = m % G_SLOTS
                pe.wait_ge(gathered[slot], (c * (TILES // G_SLOTS) + m // G_SLOTS + 1) * 2 * BT * 16)
                if ps_taken:
                    pe.wait_ge(q_hi_ready, c * TILES + m)
                for t in range(BT):
                    last = nc.tensor.transpose(tr_ps[:, P * t:P * t + P], rows[:, slot, t, :], ident[:, :])
                last.then_inc(transposed, 1)

            def bilinear(c, u):
                m, k = UNITS[u]
                if k == 0:
                    pe.wait_ge(q_ready, c * TILES + m + 1)
                pe.wait_ge(t_free, c * NU + u + 1)
                if u == 2:
                    pe.wait_ge(y_ready, START + c)
                for b in BLOCKS_OF[u]:
                    _, jj, _ = BLOCKS[b]
                    n, o = b // PIECE, b % PIECE * P
                    if b % PIECE == 0:
                        pe.wait_ge(w_lo_ready, c * NPIECE + n + 1)
                    q = (q_even, q_odd)[jj][:, m % Q_SLOTS, :]
                    dst = t_ps[u % T_SLOTS][:, jj, :]
                    nc.tensor.matmul(dst, w_hi[:, n % W_SLOTS, o:o + P], q, start=True, stop=False)
                    last = nc.tensor.matmul(dst, w_lo[:, n % W_SLOTS, o:o + P], q, start=False, stop=True)
                last.then_inc(t_ready, 1)

            def sum_group(c, first):
                group = sorted(range(first, first + GROUPS), key=lambda b: BLOCKS[b][2])
                if first % ZB == 0:
                    pe.wait_ge(z_copied, START + c * ZT + first // ZB)
                pe.wait_ge(t_free, c * NU + BLOCKS[first + GROUPS - 1][0] + 1 + T_SLOTS)
                for b in group:
                    last = sum_halves(b)
                last.then_inc(summed, GROUPS)

            def sum_halves(b):
                u, jj, half = BLOCKS[b]
                t, v = divmod(b, ZB)
                g, r = v % GROUPS, v // GROUPS
                last_block = min(NBLK, (t + 1) * ZB) - 1
                K = E if half else P
                dense_follows = t == ZT - 1 and g == 0
                return nc.tensor.matmul(z_ps[32 * g:32 * g + 32, :], strip[0:K, 30 - 2 * r:62 - 2 * r],
                                        prod[0:K, u % PROD_SLOTS, jj, :], start=r == 0,
                                        stop=b > last_block - GROUPS and not dense_follows)

            def tower(c):
                nc.tensor.matmul(z_ps[0:32, :], place[:, :], dense[:, :], start=False, stop=True).then_inc(
                    dense_placed, 1)
                for t in range(ZT):
                    pe.wait_ge(z_copied, START + c * ZT + t + 1)
                    for h in range(H1 // P):
                        last = nc.tensor.matmul(t_ps[h // 2][:, h % 2, :], w1[:, t, P * h:P * h + P], z_t[:, t, :],
                                                start=t == 0, stop=t == ZT - 1)
                        if t == ZT - 1:
                            last.then_inc(h1_ps, 1)
                for k in range(H1 // P):
                    pe.wait_ge(h1_ready, c * (H1 // P) + k + 1)
                    for h in range(H2 // P):
                        last = nc.tensor.matmul(t_ps[2][:, h, :], w2[:, k, P * h:P * h + P], h1[:, k, :],
                                                start=k == 0, stop=k == H1 // P - 1)
                        if k == H1 // P - 1:
                            last.then_inc(h2_ps, 1)
                for k in range(H2 // P):
                    pe.wait_ge(h2_ready, c * (H2 // P) + k + 1)
                    last = nc.tensor.matmul(t_ps[2][0:1, 0, :], w3[:, k:k + 1], h2[:, k, :],
                                            start=k == 0, stop=k == H2 // P - 1)
                last.then_inc(y_ps, 1)

            for m in range(HEAD_TILES):
                transpose_tile(0, m, m > 0)
            pe.wait_ge(mlp_in, 5 * 16)
            with pe.Fori(0, CHUNKS) as c:
                done = 0
                for u in range(NU):
                    for tile in prep_before.get(u, ()):
                        transpose_tile(c, tile, True)
                    if u in HEAD_AT:
                        with pe.If(c < CHUNKS - 1):
                            transpose_tile(c, TILES + HEAD_AT.index(u), True)
                    bilinear(c, u)
                    while done < NBLK and BLOCKS[done + GROUPS - 1][0] <= u - LAG:
                        sum_group(c, done)
                        done += GROUPS
                pe.wait_ge(dense_in, (c + 1) * 16)
                for b in range(done, NBLK, GROUPS):
                    sum_group(c, b)
                tower(c)


def kernel(**inputs):
    import numpy as np
    import concourse.bacc as bacc
    from concourse.bass_utils import run_bass_kernel_spmd

    tables = [np.ascontiguousarray(inputs[f"tbl_{f}"]) for f in range(FIELDS)]
    ids = np.asarray(inputs["ids"]).reshape(CHUNKS, BT, P, FIELDS)
    idx = np.ascontiguousarray(ids.transpose(2, 0, 3, 1).reshape(P, CHUNKS, FIELDS * BT))
    order = []
    for u, jj, half in BLOCKS:
        m, k = UNITS[u]
        j = 2 * m + jj
        order += [pair(2 * k, j), pair(2 * k, j) if half else pair(2 * k + 1, j)]
    weights = np.ascontiguousarray(np.asarray(inputs["L0_rec_param"])[:, order, :].reshape(E, NBLK * P))
    w_top1 = np.asarray(inputs["W_top1"])
    w1z = np.zeros((ZT, P, H1), w_top1.dtype)
    for b, (u, jj, half) in enumerate(BLOCKS):
        t, r = z_row(b)
        w1z[t, r] = w_top1[order[2 * b]]
        if not half:
            w1z[t, r + 1] = w_top1[order[2 * b + 1]]
    w1z[ZT - 1, DENSE_ROW:DENSE_ROW + DENSE] = w_top1[FIELDS * (FIELDS - 1) // 2:]

    arrays = {
        "idx": idx,
        "dense_t": np.ascontiguousarray(np.asarray(inputs["dense_ctx"]).T),
        "weights": weights,
        "w1z": np.ascontiguousarray(w1z.transpose(1, 0, 2)),
        "b1c": np.ascontiguousarray(np.asarray(inputs["b_top1"]).reshape(H1 // P, P).T),
        "w2p": np.ascontiguousarray(np.asarray(inputs["W_top2"]).reshape(H1 // P, P, H2).transpose(1, 0, 2)),
        "b2c": np.ascontiguousarray(np.asarray(inputs["b_top2"]).reshape(H2 // P, P).T),
        "w3c": np.ascontiguousarray(np.asarray(inputs["W_top3"]).reshape(H2 // P, P).T),
    }
    nc = bacc.Bacc("TRN2", target_bir_lowering=False, num_devices=1)

    def dram(name, a):
        return nc.dram_tensor(name, a.shape, mybir.dt.from_np(a.dtype), kind="ExternalInput").ap()

    table_aps = [dram(f"tbl_{f}", a) for f, a in enumerate(tables)]
    aps = {name: dram(name, a) for name, a in arrays.items()}
    out = nc.dram_tensor("y_out_dram", (1, BATCH), F32, kind="ExternalOutput").ap()
    bilinear_tower(nc, table_aps, aps["idx"], aps["dense_t"], aps["weights"], aps["w1z"], aps["b1c"], aps["w2p"],
                   aps["b2c"], aps["w3c"], out)
    arrays.update({f"tbl_{f}": a for f, a in enumerate(tables)})
    r = run_bass_kernel_spmd(nc, [arrays], core_ids=[0])
    return r.results[0]["y_out_dram"].reshape(BATCH, 1)
```

```python
from contextlib import ExitStack

import concourse.bass as bass
from concourse import mybir

F32 = mybir.dt.float32
F32R = mybir.dt.float32r
I32 = mybir.dt.int32
ALU = mybir.AluOpType
ACT = mybir.ActivationFunctionType

P = 128
E = 64
FIELDS = 40
BATCH = 2048
DENSE = 16
H1, H2 = 512, 256
TILES = FIELDS // 2
NB = 512
CHUNKS = BATCH // NB
BT = NB // P

UNITS = [(m, k) for m in range(TILES) for k in range(m + 1)]
NU = len(UNITS)
BLOCKS = [(u, jj, k == m) for u, (m, k) in enumerate(UNITS) for jj in ((0, 1) if k < m else (1,))]
NBLK = len(BLOCKS)
BLOCKS_OF = [[b for b, (v, _, _) in enumerate(BLOCKS) if v == u] for u in range(NU)]

IDX = FIELDS * BT
PIECE = 10
NPIECE = NBLK // PIECE
PW = PIECE * P
RAW_SLOTS, W_SLOTS = 2, 4
G_SLOTS = 10
Q_SLOTS = 5
T_SLOTS = 3
PROD_SLOTS = 10
LAG = 3

ZB = 64
ZT = -(-NBLK // ZB)
DENSE_ROW = 16
GROUPS = 4
SUMS = 2 * GROUPS
START = 1

HEAD_TILES = 4
HEAD_PIECES = 3
TOWER_AT = 15
HEAD_GATHERS = 10
POOL_FROM = 9
LAST = NU - TILES
LAST_BLOCK = BLOCKS_OF[LAST][0]
HEAD_AT = [LAST + 6 + 3 * t for t in range(HEAD_TILES)]
PREP_LEAD = 7
SUB_DELAY = 2


def pair(i, j):
    return i * FIELDS - i * (i + 1) // 2 + j - i - 1


def z_row(b):
    t, v = divmod(b, ZB)
    return t, 32 * (v % GROUPS) + 2 * (v // GROUPS)


def first_unit(m):
    return m * (m + 1) // 2


def units_through_piece(n):
    return BLOCKS[PIECE * (n + 1) - 1][0] + 1 if n >= 0 else 0


def sums_before(u):
    return -(-(BLOCKS_OF[u][-1] + 1) // SUMS) * SUMS if u >= 0 else 0


def prep_unit(m):
    assert HEAD_TILES ** 2 - (HEAD_TILES - 1) ** 2 >= PREP_LEAD
    return max(first_unit(s) for s in range(m) if m * m - s * s >= PREP_LEAD)


def prep_plan():
    transposes, splits = {}, {}
    for m in range(HEAD_TILES, TILES):
        transposes.setdefault(prep_unit(m), []).append(m)
        splits.setdefault(min(prep_unit(m) + SUB_DELAY, first_unit(m)), []).append(m)
    return transposes, splits


def pool_plan():
    gather_time, lead, tower_time = 20, 10, 48
    needed = {m: BLOCKS_OF[prep_unit(m)][0] for m in range(HEAD_TILES, TILES)}
    needed.update({TILES + t: LAST_BLOCK + 2 * (u - LAST) for t, u in enumerate(HEAD_AT)})
    needed.update({TILES + m: NBLK + tower_time + needed[m] for m in range(HEAD_TILES, HEAD_GATHERS)})
    tasks, start = [], float("inf")
    for m in reversed(range(HEAD_GATHERS, TILES + HEAD_GATHERS)):
        start = min(needed[m], start) - gather_time
        tasks.append((start - lead, "gather", m))
    for n in range(HEAD_PIECES, NPIECE):
        tasks.append((PIECE * (n - HEAD_PIECES) + 3, "split", n))
    return [(kind, n) for _, kind, n in sorted(tasks)]


def bilinear_tower(nc, tables, idx, dense_t, weights, w1z, b1c, w2p, b2c, w3c, out):
    prep_before, split_before = prep_plan()

    with ExitStack() as ctx:
        def sb(name, shape, dt=F32):
            return ctx.enter_context(nc.sbuf_tensor(name, shape, dt))

        def ps(name, shape):
            return ctx.enter_context(nc.psum_tensor(name, shape, F32))

        def sem(name):
            return ctx.enter_context(nc.semaphore(name))

        idx_now = sb("idx_now", [P, IDX], I32)
        rows = sb("rows", [P, G_SLOTS, BT, 2 * E])
        e_t = sb("e_t", [P, TILES, NB])
        q_even = sb("q_even", [P, Q_SLOTS, NB], F32R)
        q_odd = sb("q_odd", [P, Q_SLOTS, NB], F32R)
        w_raw = sb("w_raw", [P, RAW_SLOTS, PW])
        w_hi = sb("w_hi", [P, W_SLOTS, PW], F32R)
        w_lo = sb("w_lo", [P, W_SLOTS, PW], F32R)
        prod = sb("prod", [P, PROD_SLOTS, 2, NB])
        z_t = sb("z_t", [P, ZT, NB])
        w1 = sb("w1", [P, ZT, H1])
        w2 = sb("w2", [P, H1 // P, H2])
        w3 = sb("w3", [P, H2 // P])
        b1 = sb("b1", [P, H1 // P])
        b2 = sb("b2", [P, H2 // P])
        h1 = prod[:, 0:2, :, :].rearrange("p s a n -> p (s a) n")
        h2 = prod[:, 2, :, :]
        y = z_t[0:1, 0, :]
        dense = sb("dense", [DENSE, NB])
        ident = sb("ident", [P, P])
        strip = sb("strip", [P, 62])
        place = sb("place", [DENSE, 32])

        t_ps = [ps(f"t_ps{i}", [P, 2, NB]) for i in range(T_SLOTS)]
        z_ps = ps("z_ps", [P, NB])
        tr_ps = ps("tr_ps", [P, NB])

        consts = sem("consts")
        strip_written = sem("strip_written")
        idx_taken = sem("idx_taken")
        first_idx_in = sem("first_idx_in")
        idx_in = sem("idx_in")
        mlp_in = sem("mlp_in")
        slot_reused = sem("slot_reused")
        gathered = [sem(f"gathered{i}") for i in range(G_SLOTS)]
        raw_in = [sem(f"raw_in{i}") for i in range(RAW_SLOTS)]
        dense_in = sem("dense_in")
        w_hi_ready = sem("w_hi_ready")
        w_lo_ready = sem("w_lo_ready")
        transposed = sem("transposed")
        q_hi_ready = sem("q_hi_ready")
        q_ready = sem("q_ready")
        t_ready = sem("t_ready")
        t_free = sem("t_free")
        summed = sem("summed")
        dense_placed = sem("dense_placed")
        z_copied = sem("z_copied")
        h1_ps = sem("h1_ps")
        h1_ready = sem("h1_ready")
        h2_ps = sem("h2_ps")
        h2_ready = sem("h2_ready")
        y_ps = sem("y_ps")
        y_ready = sem("y_ready")
        y_out = sem("y_out")

        block = ctx.enter_context(nc.Block())

        @block.sync
        def _(sp):
            def load_piece(c, n):
                cols = weights[:, (n % NPIECE) * PW:(n % NPIECE + 1) * PW]
                for half in range(2):
                    sp.dma_start(w_raw[E * half:E * half + E, n % RAW_SLOTS, :], cols).then_inc(
                        raw_in[n % RAW_SLOTS], 16)

            sp.dma_start(idx_now[:, :], idx[:, 0:IDX]).then_inc(first_idx_in, 16)
            for n in range(RAW_SLOTS):
                load_piece(0, n)
            with sp.Fori(0, CHUNKS) as c:
                for n in range(RAW_SLOTS, NPIECE):
                    sp.wait_ge(w_lo_ready, c * NPIECE + n - RAW_SLOTS + 1)
                    load_piece(c, n)
                    if n == TOWER_AT:
                        with sp.If(c < 1):
                            for dst, src in ((b1[:, :], b1c), (b2[:, :], b2c), (w3[:, :], w3c),
                                             (w2[:, :, :], w2p), (w1[:, :, :], w1z)):
                                sp.dma_start(dst, src).then_inc(mlp_in, 16)
                with sp.If(c < CHUNKS - 1):
                    for n in range(NPIECE, NPIECE + RAW_SLOTS):
                        sp.wait_ge(w_lo_ready, c * NPIECE + n - RAW_SLOTS + 1)
                        load_piece(c, n)

        @block.gpsimd
        def _(pool):
            nc.gpsimd.memset(ident[:, :], 0.0).then_inc(consts, 1)
            nc.gpsimd.memset(place[:, :], 0.0).then_inc(consts, 1)
            pool.wait_ge(consts, 2)
            nc.gpsimd.affine_select(out=ident[:, :], in_=ident[:, :], compare_op=ALU.not_equal, fill=1.0,
                                    base=0, pattern=[[-1, P]], channel_multiplier=1).then_inc(consts, 1)
            nc.gpsimd.affine_select(out=place[:, :], in_=place[:, :], compare_op=ALU.not_equal, fill=1.0,
                                    base=DENSE_ROW, pattern=[[-1, 32]], channel_multiplier=1).then_inc(consts, 1)

            def gather(c, m, slot_taken):
                slot = m % G_SLOTS
                if slot_taken:
                    pool.wait_ge(transposed, c * TILES + m - G_SLOTS + 1)
                    pool.sem_inc(slot_reused, 1)
                for f in range(2):
                    for t in range(BT):
                        col = ((m % TILES) * 2 + f) * BT + t
                        nc.gpsimd.indirect_dma_start(
                            out=rows[:, slot, t, E * f:E * f + E], out_offset=None, in_=tables[(m % TILES) * 2 + f],
                            in_offset=bass.IndirectOffsetOnAxis(ap=idx_now[:, col:col + 1], axis=0),
                        ).then_inc(gathered[slot], 16)

            def split(c, n):
                if n in (HEAD_PIECES, POOL_FROM):
                    pool.wait_ge(w_lo_ready, c * NPIECE + n)
                pool.wait_ge(w_hi_ready, c * NPIECE + n + 1)
                nc.gpsimd.tensor_tensor(w_lo[:, n % W_SLOTS, :], w_raw[:, n % RAW_SLOTS, :],
                                        w_hi[:, n % W_SLOTS, :].bitcast(F32), ALU.subtract).then_inc(w_lo_ready, 1)

            plan = pool_plan()
            turn = plan.index(("gather", TILES))
            pool.wait_ge(first_idx_in, 16)
            for m in range(HEAD_GATHERS):
                gather(0, m, False)
            with pool.Fori(0, CHUNKS) as c:
                for at, (kind, n) in enumerate(plan):
                    if at == turn:
                        with pool.If(c < CHUNKS - 1):
                            for slot in range(G_SLOTS):
                                pool.wait_ge(gathered[slot], (c + 1) * (TILES // G_SLOTS) * 2 * BT * 16)
                            following = nc.s_assert_within(c + 1, 1, CHUNKS - 1)
                            pool.dma_start(idx_now[:, :], idx[:, bass.ds(following * IDX, IDX)]).then_inc(
                                idx_in, 16)
                            pool.wait_ge(idx_in, (c + 1) * 16)
                            pool.sem_inc(idx_taken, 1)
                    if kind == "split" and n < POOL_FROM:
                        with pool.If(c > 0):
                            split(c, n)
                    elif kind == "split":
                        split(c, n)
                    elif n < TILES:
                        gather(c, n, n >= G_SLOTS)
                    else:
                        with pool.If(c < CHUNKS - 1):
                            gather(c, n, True)

        @block.scalar
        def _(act):
            def round_weights(c, n, slot_taken):
                act.wait_ge(raw_in[n % RAW_SLOTS], (c * (NPIECE // RAW_SLOTS) + n // RAW_SLOTS + 1) * 32)
                if slot_taken:
                    act.wait_ge(t_ready, START + c * NU + units_through_piece(n - W_SLOTS))
                nc.scalar.activation(w_hi[:, n % W_SLOTS, :], w_raw[:, n % RAW_SLOTS, :],
                                     ACT.Copy).then_inc(w_hi_ready, 1)

            def prepare(c, m, slot_taken):
                act.wait_ge(transposed, c * TILES + m + 1)
                if m >= TILES:
                    act.wait_ge(t_free, c * NU + (LAST + m - TILES) + 1 + T_SLOTS)
                tile, slot = m % TILES, m % Q_SLOTS
                nc.scalar.activation(e_t[:, tile, :], tr_ps[:, :], ACT.Copy)
                if slot_taken:
                    act.wait_ge(t_ready, START + c * NU + first_unit(m - Q_SLOTS + 1))
                nc.scalar.activation(q_even[0:E, slot, :], tr_ps[0:E, :], ACT.Copy)
                nc.scalar.activation(q_odd[E:P, slot, :], tr_ps[E:P, :], ACT.Copy).then_inc(q_hi_ready, 1)

            def copy_z(c, t):
                if t < ZT - 1:
                    act.wait_ge(summed, START + c * NBLK + (t + 1) * ZB)
                else:
                    act.wait_ge(dense_placed, START + c + 1)
                nc.scalar.activation(z_t[:, t, :], z_ps[:, :], ACT.Copy).then_inc(z_copied, 1)

            def tower(c):
                act.wait_ge(mlp_in, 5 * 16)
                for h in range(H1 // P):
                    act.wait_ge(h1_ps, c * (H1 // P) + h + 1)
                    nc.scalar.activation(h1[:, h, :], t_ps[h // 2][:, h % 2, :], ACT.Relu,
                                         bias=b1[:, h:h + 1]).then_inc(h1_ready, 1)
                for h in range(H2 // P):
                    act.wait_ge(h2_ps, c * (H2 // P) + h + 1)
                    nc.scalar.activation(h2[:, h, :], t_ps[2][:, h, :], ACT.Relu,
                                         bias=b2[:, h:h + 1]).then_inc(h2_ready, 1)
                act.wait_ge(y_ps, c + 1)
                nc.scalar.activation(y, t_ps[2][0:1, 0, :], ACT.Copy).then_inc(y_ready, 1)
                act.wait_ge(y_ready, START + c + 1)
                act.dma_start(out[:, bass.ds(c * NB, NB)], y).then_inc(y_out, 16)
                act.wait_ge(y_out, (c + 1) * 16)

            act.sem_inc(z_copied, START)
            act.sem_inc(y_ready, START)
            for n in range(HEAD_PIECES):
                round_weights(0, n, False)
            prepare(0, 0, False)
            with act.Fori(0, CHUNKS) as c:
                act.wait_ge(dense_placed, START + c)
                act.dma_start(dense[:, :], dense_t[:, bass.ds(c * NB, NB)]).then_inc(dense_in, 16)
                for u, (m, k) in enumerate(UNITS):
                    if k == 0 and 0 < m < HEAD_TILES:
                        with act.If(c < 1):
                            prepare(c, m, False)
                    for tile in prep_before.get(u, ()):
                        prepare(c, tile, tile >= Q_SLOTS)
                    if u in HEAD_AT:
                        with act.If(c < CHUNKS - 1):
                            prepare(c, TILES + HEAD_AT.index(u), True)
                    for b in BLOCKS_OF[u]:
                        if b % PIECE == 0:
                            n = b // PIECE + HEAD_PIECES
                            if n < NPIECE:
                                round_weights(c, n, True)
                            elif n < NPIECE + HEAD_PIECES - 1:
                                with act.If(c < CHUNKS - 1):
                                    round_weights(c, n, True)
                    for b in BLOCKS_OF[max(u - LAG - 1, 0)]:
                        if u > LAG and b % ZB == ZB - 1:
                            copy_z(c, b // ZB)
                copy_z(c, ZT - 1)
                with act.If(c < CHUNKS - 1):
                    round_weights(c, NPIECE + HEAD_PIECES - 1, True)
                tower(c)

        @block.vector
        def _(dve):
            dve.sem_inc(t_free, T_SLOTS)
            nc.vector.memset(strip[:, :], 0.0).then_inc(strip_written, 1)
            dve.wait_ge(strip_written, 1)
            nc.vector.memset(strip[0:E, 30:31], 1.0).then_inc(strip_written, 1)
            nc.vector.memset(strip[E:P, 31:32], 1.0).then_inc(strip_written, 1)

            def remainders(c, m):
                tile, slot = m % TILES, m % Q_SLOTS
                dve.wait_ge(q_hi_ready, c * TILES + m + 1)
                nc.vector.tensor_tensor(q_even[E:P, slot, :], e_t[0:E, tile, :],
                                        q_even[0:E, slot, :].bitcast(F32), ALU.subtract)
                nc.vector.tensor_tensor(q_odd[0:E, slot, :], e_t[E:P, tile, :],
                                        q_odd[E:P, slot, :].bitcast(F32), ALU.subtract).then_inc(q_ready, 1)

            def split(c, n):
                dve.wait_ge(w_hi_ready, c * NPIECE + n + 1)
                nc.vector.tensor_tensor(w_lo[:, n % W_SLOTS, :], w_raw[:, n % RAW_SLOTS, :],
                                        w_hi[:, n % W_SLOTS, :].bitcast(F32), ALU.subtract).then_inc(w_lo_ready, 1)

            for n in range(HEAD_PIECES):
                split(0, n)
            remainders(0, 0)
            with dve.Fori(0, CHUNKS) as c:
                for u, (m, k) in enumerate(UNITS):
                    if k == 0 and 0 < m < HEAD_TILES:
                        with dve.If(c < 1):
                            remainders(c, m)
                    for tile in split_before.get(u, ()):
                        remainders(c, tile)
                    for b in BLOCKS_OF[u]:
                        n = b // PIECE + HEAD_PIECES
                        if b % PIECE == PIECE - 2 and n < POOL_FROM:
                            with dve.If(c < 1):
                                split(c, n)
                    dve.wait_ge(t_ready, START + c * NU + u + 1)
                    dve.wait_ge(summed, START + c * NBLK + sums_before(u - PROD_SLOTS))
                    dst, src = prod[:, u % PROD_SLOTS, :, :], t_ps[u % T_SLOTS]
                    if k < m:
                        nc.vector.tensor_tensor(dst, src[:, :, :],
                                                e_t[:, k, :].unsqueeze(1).broadcast_to([P, 2, NB]),
                                                ALU.mult).then_inc(t_free, 1)
                    else:
                        nc.vector.tensor_tensor(dst[0:E, 1, :], src[0:E, 1, :], e_t[0:E, k, :],
                                                ALU.mult).then_inc(t_free, 1)
                with dve.If(c < CHUNKS - 1):
                    dve.wait_ge(w_lo_ready, (c + 1) * NPIECE)
                    for n in range(NPIECE, NPIECE + HEAD_PIECES - 1):
                        split(c, n)
                    for m in range(TILES, TILES + HEAD_TILES):
                        remainders(c, m)
                    split(c, NPIECE + HEAD_PIECES - 1)

        @block.tensor
        def _(pe):
            for s in (t_ready, summed, dense_placed):
                pe.sem_inc(s, START)
            pe.wait_ge(consts, 4)
            pe.wait_ge(strip_written, 3)

            def transpose_tile(c, m, ps_taken):
                slot = m % G_SLOTS
                pe.wait_ge(gathered[slot], (c * (TILES // G_SLOTS) + m // G_SLOTS + 1) * 2 * BT * 16)
                if ps_taken:
                    pe.wait_ge(q_hi_ready, c * TILES + m)
                for t in range(BT):
                    last = nc.tensor.transpose(tr_ps[:, P * t:P * t + P], rows[:, slot, t, :], ident[:, :])
                last.then_inc(transposed, 1)

            def bilinear(c, u):
                m, k = UNITS[u]
                if k == 0:
                    pe.wait_ge(q_ready, c * TILES + m + 1)
                pe.wait_ge(t_free, c * NU + u + 1)
                if u == 2:
                    pe.wait_ge(y_ready, START + c)
                for b in BLOCKS_OF[u]:
                    _, jj, _ = BLOCKS[b]
                    n, o = b // PIECE, b % PIECE * P
                    if b % PIECE == 0:
                        pe.wait_ge(w_lo_ready, c * NPIECE + n + 1)
                    q = (q_even, q_odd)[jj][:, m % Q_SLOTS, :]
                    dst = t_ps[u % T_SLOTS][:, jj, :]
                    nc.tensor.matmul(dst, w_hi[:, n % W_SLOTS, o:o + P], q, start=True, stop=False)
                    last = nc.tensor.matmul(dst, w_lo[:, n % W_SLOTS, o:o + P], q, start=False, stop=True)
                last.then_inc(t_ready, 1)

            def sum_group(c, first):
                group = list(range(first, first + SUMS))
                if BLOCKS[first][2]:
                    group[:2] = first + 1, first
                if first % ZB == 0:
                    pe.wait_ge(z_copied, START + c * ZT + first // ZB)
                pe.wait_ge(t_free, c * NU + BLOCKS[first + SUMS - 1][0] + 1 + T_SLOTS)
                for b in group:
                    last = sum_halves(b)
                last.then_inc(summed, SUMS)

            def sum_halves(b):
                u, jj, half = BLOCKS[b]
                t, v = divmod(b, ZB)
                g, r = v % GROUPS, v // GROUPS
                last_block = min(NBLK, (t + 1) * ZB) - 1
                K = E if half else P
                dense_follows = t == ZT - 1 and g == 0
                return nc.tensor.matmul(z_ps[32 * g:32 * g + 32, :], strip[0:K, 30 - 2 * r:62 - 2 * r],
                                        prod[0:K, u % PROD_SLOTS, jj, :], start=r == 0,
                                        stop=b > last_block - GROUPS and not dense_follows)

            def tower(c):
                nc.tensor.matmul(z_ps[0:32, :], place[:, :], dense[:, :], start=False, stop=True).then_inc(
                    dense_placed, 1)
                for t in range(ZT):
                    pe.wait_ge(z_copied, START + c * ZT + t + 1)
                    for h in range(H1 // P):
                        last = nc.tensor.matmul(t_ps[h // 2][:, h % 2, :], w1[:, t, P * h:P * h + P], z_t[:, t, :],
                                                start=t == 0, stop=t == ZT - 1)
                        if t == ZT - 1:
                            last.then_inc(h1_ps, 1)
                for k in range(H1 // P):
                    pe.wait_ge(h1_ready, c * (H1 // P) + k + 1)
                    for h in range(H2 // P):
                        last = nc.tensor.matmul(t_ps[2][:, h, :], w2[:, k, P * h:P * h + P], h1[:, k, :],
                                                start=k == 0, stop=k == H1 // P - 1)
                        if k == H1 // P - 1:
                            last.then_inc(h2_ps, 1)
                for k in range(H2 // P):
                    pe.wait_ge(h2_ready, c * (H2 // P) + k + 1)
                    last = nc.tensor.matmul(t_ps[2][0:1, 0, :], w3[:, k:k + 1], h2[:, k, :],
                                            start=k == 0, stop=k == H2 // P - 1)
                last.then_inc(y_ps, 1)

            transpose_tile(0, 0, False)
            with pe.Fori(0, CHUNKS) as c:
                done = 0
                for u, (m, k) in enumerate(UNITS):
                    if k == 0 and 0 < m < HEAD_TILES:
                        with pe.If(c < 1):
                            transpose_tile(c, m, True)
                    for tile in prep_before.get(u, ()):
                        transpose_tile(c, tile, True)
                    if u in HEAD_AT:
                        with pe.If(c < CHUNKS - 1):
                            transpose_tile(c, TILES + HEAD_AT.index(u), True)
                    bilinear(c, u)
                    while done < NBLK and BLOCKS[done + SUMS - 1][0] <= u - LAG:
                        sum_group(c, done)
                        done += SUMS
                pe.wait_ge(mlp_in, 5 * 16)
                pe.wait_ge(dense_in, (c + 1) * 16)
                for b in range(done, NBLK, SUMS):
                    sum_group(c, b)
                tower(c)


def kernel(**inputs):
    import numpy as np
    import concourse.bacc as bacc
    from concourse.bass_utils import run_bass_kernel_spmd

    tables = [np.ascontiguousarray(inputs[f"tbl_{f}"]) for f in range(FIELDS)]
    ids = np.asarray(inputs["ids"]).reshape(CHUNKS, BT, P, FIELDS)
    idx = np.ascontiguousarray(ids.transpose(2, 0, 3, 1).reshape(P, CHUNKS * IDX))
    order = []
    for u, jj, half in BLOCKS:
        m, k = UNITS[u]
        j = 2 * m + jj
        order += [pair(2 * k, j), pair(2 * k, j) if half else pair(2 * k + 1, j)]
    weights = np.ascontiguousarray(np.asarray(inputs["L0_rec_param"])[:, order, :].reshape(E, NBLK * P))
    w_top1 = np.asarray(inputs["W_top1"])
    w1z = np.zeros((ZT, P, H1), w_top1.dtype)
    for b, (u, jj, half) in enumerate(BLOCKS):
        t, r = z_row(b)
        w1z[t, r] = w_top1[order[2 * b]]
        if not half:
            w1z[t, r + 1] = w_top1[order[2 * b + 1]]
    w1z[ZT - 1, DENSE_ROW:DENSE_ROW + DENSE] = w_top1[FIELDS * (FIELDS - 1) // 2:]

    arrays = {
        "idx": idx,
        "dense_t": np.ascontiguousarray(np.asarray(inputs["dense_ctx"]).T),
        "weights": weights,
        "w1z": np.ascontiguousarray(w1z.transpose(1, 0, 2)),
        "b1c": np.ascontiguousarray(np.asarray(inputs["b_top1"]).reshape(H1 // P, P).T),
        "w2p": np.ascontiguousarray(np.asarray(inputs["W_top2"]).reshape(H1 // P, P, H2).transpose(1, 0, 2)),
        "b2c": np.ascontiguousarray(np.asarray(inputs["b_top2"]).reshape(H2 // P, P).T),
        "w3c": np.ascontiguousarray(np.asarray(inputs["W_top3"]).reshape(H2 // P, P).T),
    }
    nc = bacc.Bacc("TRN2", target_bir_lowering=False, num_devices=1)

    def dram(name, a):
        return nc.dram_tensor(name, a.shape, mybir.dt.from_np(a.dtype), kind="ExternalInput").ap()

    table_aps = [dram(f"tbl_{f}", a) for f, a in enumerate(tables)]
    aps = {name: dram(name, a) for name, a in arrays.items()}
    out = nc.dram_tensor("y_out_dram", (1, BATCH), F32, kind="ExternalOutput").ap()
    bilinear_tower(nc, table_aps, aps["idx"], aps["dense_t"], aps["weights"], aps["w1z"], aps["b1c"], aps["w2p"],
                   aps["b2c"], aps["w3c"], out)
    arrays.update({f"tbl_{f}": a for f, a in enumerate(tables)})
    r = run_bass_kernel_spmd(nc, [arrays], core_ids=[0])
    return r.results[0]["y_out_dram"].reshape(BATCH, 1)
```
